# Optimizing a Trainium2 kernel written in Bass

```python
import numpy as np
import jax
import jax.numpy as jnp

def _softmax(x, axis=-1):
    return jax.nn.softmax(x, axis=axis)

def _gelu(x):
    return jax.nn.gelu(x, approximate=True)

def _silu(x):
    return jax.nn.silu(x)

def _sigmoid(x):
    return jax.nn.sigmoid(x)

def _layernorm(x, axis=-1, eps=1e-05):
    m = jnp.mean(x, axis=axis, keepdims=True)
    v = jnp.var(x, axis=axis, keepdims=True)
    return (x - m) / jnp.sqrt(v + eps)

def _scatter_add(tgt, idx, src, axis=0):
    return tgt.at[idx].add(src)

def _segment_sum(src, seg, n):
    return jax.ops.segment_sum(src, seg, n)
kernel_name = 'mk_gnn_resnorm_d2_gnn_r8_80f372'

def setup_inputs(seed: int=0):
    np.random.seed(seed)
    _w = jnp.asarray

    def _rec_inputs():
        import jax
        import jax.numpy as jnp
        _gk = jax.random.key(seed)
        x = -0.0003713 + 1 * jax.random.normal(jax.random.fold_in(_gk, 1), (6250, 256), jnp.float32)
        _s = jax.random.randint(jax.random.fold_in(_gk, 2), (50000,), 0, 6250, jnp.int32)
        _d = jax.random.randint(jax.random.fold_in(_gk, 3), (50000,), 0, 6250, jnp.int32)
        _loop = jnp.arange(6250, dtype=jnp.int32)
        src = jnp.concatenate([_s, _d, _loop])
        dst = jnp.concatenate([_d, _s, _loop])
        _o = jnp.argsort(dst, stable=True)
        src = src[_o]
        dst = dst[_o]
        edge_attr_8 = 0.000735704 + 1.0001 * jax.random.normal(jax.random.fold_in(_gk, 12), (106250, 8), jnp.float32)
        edge_attr_8_n2 = 0.000735704 + 1.0001 * jax.random.normal(jax.random.fold_in(_gk, 13), (106250, 8), jnp.float32)
        return (x, src, dst, edge_attr_8, edge_attr_8_n2)
    x, src, dst, edge_attr_8, edge_attr_8_n2 = _rec_inputs()

    def _L0_gnn_setup():
        import jax, jax.numpy as jnp
        import numpy as np
        N_NODES = 6250
        N_EDGES = 100000
        D_IN = 256
        D_OUT = 64
        N_HEADS = 4
        key = jax.random.key(seed)
        k1, k2, k3, k4 = jax.random.split(key, 4)
        x = jax.random.normal(k1, (N_NODES, D_IN), dtype=jnp.float32)
        W = jax.random.normal(k2, (N_HEADS, D_IN, D_OUT), dtype=jnp.float32) * np.sqrt(2.0 / (D_IN + D_OUT))
        a = jax.random.normal(k3, (N_HEADS, 2 * D_OUT), dtype=jnp.float32) * np.sqrt(2.0 / (2 * D_OUT + 1))
        edge_index = jax.random.randint(k4, (N_EDGES, 2), 0, N_NODES, dtype=jnp.int32)
        return {'x': x, 'W': W, 'a': a, 'edge_index': edge_index}
    _L0_gnn_all = _L0_gnn_setup()
    _L0_gnn_in = {k: v for k, v in _L0_gnn_all.items() if k in ('W', 'a')}
    del _L0_gnn_all

    def _L1_gnn_setup():
        import jax, jax.numpy as jnp
        import numpy as np
        N, E, D, H = (2500, 40000, 256, 8)
        DH = D // H

        def layer_norm(x, g, b, eps=1e-05):
            mu = x.mean(-1, keepdims=True)
            var = ((x - mu) ** 2).mean(-1, keepdims=True)
            return (x - mu) * jax.lax.rsqrt(var + eps) * g + b
        key = jax.random.key(seed)
        ks = jax.random.split(key, 10)
        s = 0.02
        return {'triplet_h': jax.random.normal(ks[0], (N, D), jnp.float32), 'dist_attn': jax.random.normal(ks[1], (E, H), jnp.float32), 'path_attn': jax.random.normal(ks[2], (E, H), jnp.float32), 'src': jax.random.randint(ks[3], (E,), 0, N), 'dst': jax.random.randint(ks[4], (E,), 0, N), 'ln1_g': jnp.ones((D,), jnp.float32), 'ln1_b': jnp.zeros((D,), jnp.float32), 'qkv_w': jax.random.normal(ks[5], (D, 3 * D), jnp.float32) * s, 'qkv_b': jnp.zeros((3 * D,), jnp.float32), 'res_ln_g': jnp.ones((D,), jnp.float32), 'res_ln_b': jnp.zeros((D,), jnp.float32), 'inproj_w': jax.random.normal(ks[6], (D, D), jnp.float32) * s, 'inproj_b': jnp.zeros((D,), jnp.float32), 'ffn1_w': jax.random.normal(ks[7], (D, 4 * D), jnp.float32) * s, 'ffn1_b': jnp.zeros((4 * D,), jnp.float32), 'ffn2_w': jax.random.normal(ks[8], (4 * D, D), jnp.float32) * s, 'ffn2_b': jnp.zeros((D,), jnp.float32)}
    _L1_gnn_all = _L1_gnn_setup()
    _L1_gnn_in = {k: v for k, v in _L1_gnn_all.items() if k in ('ln1_g', 'ln1_b', 'qkv_w', 'qkv_b', 'res_ln_g', 'res_ln_b', 'inproj_w', 'inproj_b', 'ffn1_w', 'ffn1_b', 'ffn2_w', 'ffn2_b')}
    del _L1_gnn_all
    return {'x': x, 'src': src, 'dst': dst, 'edge_attr_8': edge_attr_8, 'edge_attr_8_n2': edge_attr_8_n2, 'L0_gnn_W': _L0_gnn_in['W'], 'L0_gnn_a': _L0_gnn_in['a'], 'L1_gnn_ln1_g': _L1_gnn_in['ln1_g'], 'L1_gnn_ln1_b': _L1_gnn_in['ln1_b'], 'L1_gnn_qkv_w': _L1_gnn_in['qkv_w'], 'L1_gnn_qkv_b': _L1_gnn_in['qkv_b'], 'L1_gnn_res_ln_g': _L1_gnn_in['res_ln_g'], 'L1_gnn_res_ln_b': _L1_gnn_in['res_ln_b'], 'L1_gnn_inproj_w': _L1_gnn_in['inproj_w'], 'L1_gnn_inproj_b': _L1_gnn_in['inproj_b'], 'L1_gnn_ffn1_w': _L1_gnn_in['ffn1_w'], 'L1_gnn_ffn1_b': _L1_gnn_in['ffn1_b'], 'L1_gnn_ffn2_w': _L1_gnn_in['ffn2_w'], 'L1_gnn_ffn2_b': _L1_gnn_in['ffn2_b']}

def reference(x, src, dst, edge_attr_8, edge_attr_8_n2, L0_gnn_W, L0_gnn_a, L1_gnn_ln1_g, L1_gnn_ln1_b, L1_gnn_qkv_w, L1_gnn_qkv_b, L1_gnn_res_ln_g, L1_gnn_res_ln_b, L1_gnn_inproj_w, L1_gnn_inproj_b, L1_gnn_ffn1_w, L1_gnn_ffn1_b, L1_gnn_ffn2_w, L1_gnn_ffn2_b):
    import jax
    import jax.numpy as jnp

    def _L0_gnn_ref(x, W, a, edge_index):
        import jax, jax.numpy as jnp
        import numpy as np
        N_NODES = 6250
        N_EDGES = 100000
        D_IN = 256
        D_OUT = 64
        N_HEADS = 4
        rows = edge_index[:, 0]
        cols = edge_index[:, 1]
        h = jnp.einsum('nd,hdo->hno', x, W)
        a1, a2 = (a[:, :D_OUT], a[:, D_OUT:])
        s1 = jnp.einsum('hno,ho->hn', h, a1)
        s2 = jnp.einsum('hno,ho->hn', h, a2)
        e = jax.nn.leaky_relu(s1[:, rows] + s2[:, cols], negative_slope=0.2)
        seg_max = jax.vmap(lambda v: jax.ops.segment_max(v, rows, num_segments=N_NODES))(e)
        ex = jnp.exp(e - seg_max[:, rows])
        seg_sum = jax.vmap(lambda v: jax.ops.segment_sum(v, rows, num_segments=N_NODES))(ex)
        alpha = ex / seg_sum[:, rows]
        msg = alpha[:, :, None] * h[:, cols]
        out = jax.vmap(lambda m: jax.ops.segment_sum(m, rows, num_segments=N_NODES))(msg)
        out = jax.nn.relu(out)
        return jnp.transpose(out, (1, 0, 2)).reshape(N_NODES, N_HEADS * D_OUT)

    def _L1_gnn_ref(triplet_h, dist_attn, path_attn, src, dst, ln1_g, ln1_b, qkv_w, qkv_b, res_ln_g, res_ln_b, inproj_w, inproj_b, ffn1_w, ffn1_b, ffn2_w, ffn2_b):
        import jax, jax.numpy as jnp
        import numpy as np
        N, E, D, H = (2500, 40000, 256, 8)
        DH = D // H

        def layer_norm(x, g, b, eps=1e-05):
            mu = x.mean(-1, keepdims=True)
            var = ((x - mu) ** 2).mean(-1, keepdims=True)
            return (x - mu) * jax.lax.rsqrt(var + eps) * g + b
        n, d = triplet_h.shape
        h = dist_attn.shape[1]
        dh = d // h
        scale = d ** (-0.5)
        nh = layer_norm(triplet_h, ln1_g, ln1_b)
        qkv = (nh @ qkv_w + qkv_b).reshape(n, 3, h, dh)
        q = qkv[:, 0] * scale
        k = qkv[:, 1]
        v = qkv[:, 2]
        logits = jnp.einsum('ehd,ehd->eh', q[src], k[dst]) + dist_attn + path_attn
        m = jax.ops.segment_max(logits, dst, num_segments=n)
        p = jnp.exp(logits - m[dst])
        z = jax.ops.segment_sum(p, dst, num_segments=n)
        sa = p / z[dst]
        he = (v[src] * sa[:, :, None]).reshape(-1, d)
        agg = jax.ops.segment_sum(he, dst, num_segments=n)
        x = triplet_h + (agg @ inproj_w + inproj_b)
        y = layer_norm(x, res_ln_g, res_ln_b)
        y = jax.nn.gelu(y @ ffn1_w + ffn1_b, approximate=False) @ ffn2_w + ffn2_b
        return x + y
    edge_index_t = jnp.stack([src, dst], axis=1)
    x = _layernorm(x + _L0_gnn_ref(x, L0_gnn_W, L0_gnn_a, edge_index_t), axis=-1)
    x = _layernorm(x + _L1_gnn_ref(x, edge_attr_8, edge_attr_8_n2, src, dst, L1_gnn_ln1_g, L1_gnn_ln1_b, L1_gnn_qkv_w, L1_gnn_qkv_b, L1_gnn_res_ln_g, L1_gnn_res_ln_b, L1_gnn_inproj_w, L1_gnn_inproj_b, L1_gnn_ffn1_w, L1_gnn_ffn1_b, L1_gnn_ffn2_w, L1_gnn_ffn2_b), axis=-1)
    return x

_drawn_inputs = setup_inputs


def setup_inputs(seed=0):
    import zlib

    import numpy as np

    out = dict(_drawn_inputs(seed))
    spreads = {'L1_gnn_ln1_g': (1.0, 0.6),
     'L1_gnn_ln1_b': (0.0, 0.8),
     'L1_gnn_qkv_b': (0.0, 0.491),
     'L1_gnn_res_ln_g': (1.0, 0.6),
     'L1_gnn_res_ln_b': (0.0, 0.8),
     'L1_gnn_inproj_b': (0.0, 0.1),
     'L1_gnn_ffn1_b': (0.0, 0.437),
     'L1_gnn_ffn2_b': (0.0, 0.1)}
    factors = {'edge_attr_8': 3.682, 'edge_attr_8_n2': 3.693}
    for name, (base, spread) in spreads.items():
        noise = np.random.default_rng([zlib.crc32(name.encode()), seed]).standard_normal(out[name].shape)
        drawn = base * np.exp(spread * noise) if base else spread * noise
        out[name] = jnp.asarray(drawn.astype(out[name].dtype))
    for name, factor in factors.items():
        out[name] = (out[name] * factor).astype(out[name].dtype)
    return out
```

```python
import math

import concourse.bass as bass
from concourse import mybir
from contextlib import ExitStack

P = 128
N = 6250
E = 106250
D = 256
HI = -(-N // P)
BLOCKS = HI + 1
ROWS = BLOCKS * P
PADKEY = HI * P
LANE = -(-E // P)
TILES = -(-LANE // 8) * 8
LASTLANE = E - (P - 1) * LANE
GROUP = 4
GROUPS = TILES // GROUP
HB = 16
PARTS = 3
R = 3
G = PARTS * R
RUN = 4
SLOTS = RUN * G
DIV = -(-65536 // G)
LOWEST = -1.0e30
OFF_TABLE = 1.0e6
EPS = 1e-5

H0, W0 = 4, 268
H1, W1 = 8, 520
S2, S1 = 260, 264
REC = 9
F = 1024


def build(nc, x, src, dst, attr_a, attr_b, W, a, ln1_g, ln1_b, qkv_w, qkv_b, res_g, res_b,
          in_w, in_b, f1_w, f1_b, f2_w, f2_b, out):
    f32, bf16, i32 = mybir.dt.float32, mybir.dt.bfloat16, mybir.dt.int32
    ALU, ACT, AX = mybir.AluOpType, mybir.ActivationFunctionType, mybir.AxisListType.X
    ctx = ExitStack()
    with ctx:
        def sb(name, shape, dt=f32):
            return ctx.enter_context(nc.sbuf_tensor(name, shape, dt))

        def sem(name):
            return ctx.enter_context(nc.semaphore(name))

        def dram(name, shape, dt=f32):
            return nc.dram_tensor(name, shape, dt, kind="Internal").ap()

        bank = [ctx.enter_context(nc.psum_tensor(f"bank{i}", [P, 512], f32)) for i in range(8)]

        neighbours = dram("neighbours", [E + SLOTS, 1])
        order = [dram(f"order{l}", [ROWS, 4]) for l in (0, 1)]
        records = dram("records", [(P + 1) * LANE, REC])
        table = [dram("rows0", [ROWS, W0]), dram("rows1", [ROWS, W1])]
        resorted = dram("resorted", [E, REC])
        own1 = dram("own1", [ROWS, 2 * D])

        sums = sb("sums", [P, BLOCKS, 264])
        room = [0]

        def early(shape, dt=f32):
            size = math.prod(shape[1:]) * (2 if dt == bf16 else 4) // 4
            flat = sums[:, :, :].rearrange("p a b -> p (a b)")[:, room[0]:room[0] + size]
            room[0] += size
            flat = flat.bitcast(dt) if dt != f32 else flat
            return flat.rearrange("p (a b) -> p a b", b=shape[2])

        identf, identb = sb("identf", [P, P]), sb("identb", [P, P], bf16)
        before = sb("before", [P, P])
        beforeb, notbeforeb = sb("beforeb", [P, P], bf16), sb("notbeforeb", [P, P], bf16)
        earlier = sb("earlier", [P, 2 * P])
        onesb = sb("onesb", [P, P], bf16)
        counti, countb, countf = sb("counti", [P, P], i32), sb("countb", [P, P], bf16), sb("countf", [P, P])
        nodei = sb("nodei", [P, BLOCKS], i32)
        lane_end = sb("lane_end", [P, 1], i32)
        drops, dropped = sb("drops", [P, 1]), sb("dropped", [P, 1])
        unsorted = sb("unsorted", [1, 1], i32)
        zrow = sb("zrow", [1, SLOTS])
        zrec = sb("zrec", [1, SLOTS * REC])
        ones128 = sb("ones128", [P, P])

        keyi = [early([P, 1, TILES + GROUP], i32)[:, 0, :] for l in (0, 1)]
        keyf = [sb(f"keyf{l}", [P, TILES + GROUP]) for l in (0, 1)]
        hib = [sb(f"hib{l}", [P, TILES + GROUP], bf16) for l in (0, 1)]
        lob = [sb(f"lob{l}", [P, TILES + GROUP], bf16) for l in (0, 1)]
        padadd = sb("padadd", [P, TILES + GROUP])
        halfi = padadd[:, :].bitcast(i32)

        hA = [early([P, HB, HI], bf16) for h in range(2)]
        hB = [early([P, HB, P], bf16) for h in range(2)]
        zerob = sb("zerob", [P, P], bf16)
        degree, upto, first = (sb(n, [HI, P]) for n in ("degree", "upto", "first0"))
        blockbase = sb("blockbase", [HI, 1])
        firsts = [first, sb("first1", [HI, P])]

        rec = [sb(f"rec{l}", [P, BLOCKS, 4]) for l in (0, 1)]
        degkey, degkeyb = sb("degkey", [P, BLOCKS]), sb("degkeyb", [P, BLOCKS], bf16)
        degone = early([P, BLOCKS, P], bf16)
        degincl, degbase = sb("degincl", [P, P]), sb("degbase", [P, P])
        place, placei = sb("place", [P, BLOCKS]), [sb(f"placei{l}", [P, BLOCKS], i32) for l in (0, 1)]
        bt = [sb(f"bt{l}", [P, BLOCKS + 1, 4]) for l in (0, 1)]
        blockmax = sb("blockmax", [BLOCKS, 1])
        mrow = sb("mrow", [1, 4, BLOCKS])
        mint = sb("mint", [1, 2, BLOCKS], i32)
        meta = [sb(f"meta{l}", [1, 3, BLOCKS], i32) for l in (0, 1)]

        oneA = [sb(f"oneA{h}", [P, GROUP, HI], bf16) for h in range(2)]
        oneB = [sb(f"oneB{h}", [P, GROUP, P], bf16) for h in range(2)]
        keycol = [sb(f"keycol{h}", [P, 2, GROUP], bf16) for h in range(2)]
        oneAT = [sb(f"oneAT{h}", [HI, GROUP * P]) for h in range(2)]
        count = [sb(f"count{h}", [HI, P]) for h in range(2)]
        junk = sb("junk", [P, 4 * GROUP, 2 * P], bf16)
        rank = [sb(f"rank{h}", [P, GROUP]) for h in range(2)]
        basis = [sb(f"basis{h}", [P, GROUP]) for h in range(2)]
        placef = [sb(f"placef{h}", [P, GROUP]) for h in range(2)]
        target = [sb(f"target{h}", [P, GROUP], i32) for h in range(2)]
        payload = [sb(f"payload{h}", [P, GROUP]) for h in range(2)]

        RCH = TILES // 8
        attr1, attr2 = ([early([P, RCH, 8]) for h in range(2)] for n in "ab")
        recs = [early([P, RCH, REC]) for h in range(2)]
        rec_tiles = [(8 * RCH * 0 + c * RCH, min(LANE, (c + 1) * RCH) - c * RCH) for c in range(8)]

        wext = sb("wext", [P, 2, 264])
        qkv_sb, in_sb = sb("qkv_sb", [P, 2, 3 * D]), sb("in_sb", [P, 2, D])
        f1_sb, f2_sb = sb("f1_sb", [P, 2, F]), sb("f2_sb", [P, 8, D])
        qkv_bias, in_bias, f2_bias = sb("qkv_bias", [P, 3 * D]), sb("in_bias", [P, D]), sb("f2_bias", [P, D])
        f1_bias = sb("f1_bias", [P, 8])
        lncol = sb("lncol", [P, 4, 2])
        eps_sb = sb("eps_sb", [P, 1])


        V = [sb(f"V{k}", [P, (R + 1) * W1]) for k in range(PARTS)]
        weighted = [sb(f"weighted{k}", [P, R + 1, 264]) for k in range(PARTS)]
        logits = [sb(f"logits{k}", [P, (R + 1) * 8]) for k in range(PARTS)]
        shifted = [sb(f"shifted{k}", [P, (R + 1) * 8]) for k in range(PARTS)]
        probs = [sb(f"probs{k}", [P, (R + 1) * 8]) for k in range(PARTS)]
        qk = sb("qk", [P, R * D])
        runs = [sb(f"runs{h}", [P, SLOTS * REC]) for h in range(2)]
        more = sb("more", [P, SLOTS * REC])
        self_rows = [sb(f"self{h}", [P, 2 * D]) for h in range(2)]
        own = sb("own", [P, D])
        degnow, mask, attrm = sb("degnow", [P, 1]), sb("mask", [P, SLOTS]), sb("attrm", [P, SLOTS, 8])
        first_at, node_at = ([sb(f"{n}{h}", [P, 1], i32) for h in range(2)] for n in ("first_at", "node_at"))
        raw_at = [sb(f"raw_at{h}", [P, 1], i32) for h in range(2)]
        firstf, more_at = sb("firstf", [P, 1]), sb("more_at", [P, 1], i32)
        ids = sb("ids", [P, SLOTS], i32)
        ids_part = [sb(f"ids_part{k}", [P, R], i32) for k in range(PARTS)]

        norm = sb("norm", [P, 4, 8])
        aggn, pre = sb("aggn", [P, D]), sb("pre", [P, D])
        st, mv, std = sb("st", [P, 3, 6]), sb("mv", [P, 3, 2]), sb("std", [P, 3, 2])
        zn, tT = sb("zn", [P, D]), sb("tT", [P, 2, P])
        xg = [sb(f"xg{h}", [P, 2 * D]) for h in range(2)]
        qv = [sb(f"qv{h}", [P, W1]) for h in range(2)]
        kx = [sb(f"kx{h}", [P, 2 * D]) for h in range(2)]
        xt = [xg[h][:, 0:D] for h in range(2)]
        xT = [kx[h][:, 0:D].rearrange("p (c n) -> p c n", c=2) for h in range(2)]
        hrow = [qv[h][:, 0:W0] for h in range(2)]
        gT = sb("gT", [P, 8, P])
        a_all, wprod = gT[:, 0:4, :], gT[:, 4:6, :].rearrange("p a (b o) -> p (a b) o", o=64)
        mid = sb("mid", [P, D])
        outrow = [sb(f"outrow{h}", [P, D]) for h in range(2)]

        consts_ready, iotas_ready, masks_ready = sem("consts_ready"), sem("iotas_ready"), sem("masks_ready")
        keys_padded, keys_loaded = sem("keys_padded"), [sem("src_loaded"), sem("dst_loaded")]
        setup_chain = sem("setup_chain")
        halves_ready = sem("halves_ready")
        hist_onehots = [sem("hist_onehots0"), sem("hist_onehots1")]
        hist_taken = [sem("hist_taken0"), sem("hist_taken1")]
        hist_done = sem("hist_done")
        totals_ready, base_ready, tables_ready, tables_turned = (
            sem(n) for n in ("totals_ready", "base_ready", "tables_ready", "tables_turned"))
        deg_onehots, deg_hist, degbase_ready, degsum_ready, degplace_ready, places_ready = (
            sem(n) for n in ("deg_onehots", "deg_hist", "degbase_ready", "degsum_ready",
                             "degplace_ready", "places_ready"))
        order_written = [sem("order_written0"), sem("order_written1")]
        order_loaded = [sem("order_loaded0"), sem("order_loaded1")]
        turned_degree, blockmax_ready, maxrow_ready = (
            sem(n) for n in ("turned_degree", "blockmax_ready", "maxrow_ready"))
        meta_ready = [sem("meta_ready0"), sem("meta_ready1")]
        waits_done = sem("waits_done")
        waits_done_dve = sem("waits_done_dve")
        c_res = sem("c_res")
        pad_written = sem("pad_written")
        seed_taken = sem("seed_taken")

        def pair(name):
            return [sem(f"{name}{h}") for h in range(2)]
        onehots_ready, turned, turned_copied, keyrows_ready = (
            pair(n) for n in ("onehots_ready", "turned", "turned_copied", "keyrows_ready"))
        targets_ready, scattered = pair("targets_ready"), pair("scattered")
        count_ready, count_copied, lookup_ready, looked_up, chain_rank = (
            sem(n) for n in ("count_ready", "count_copied", "lookup_ready", "looked_up", "chain_rank"))

        weights_loaded, wext_ready = sem("weights_loaded"), sem("wext_ready")
        attrs_loaded, recs_ready, recs_stored = pair("attrs_loaded"), pair("recs_ready"), pair("recs_stored")
        recpad_written = sem("recpad_written")
        group_loaded, resorted_moved = pair("group_loaded"), sem("resorted_moved")
        h_moved = pair("h_moved")
        x_loaded, x_turned, xT_copied, h_ready, hrow_ready, hrow_stored = (
            pair(n) for n in ("x_loaded", "x_turned", "xT_copied", "h_ready", "hrow_ready", "hrow_stored"))

        def layered(name):
            return [sem(f"{name}_L{l}") for l in (0, 1)]
        run_arrived, self_arrived = ([[sem(f"{n}{l}_{h}") for h in range(2)] for l in (0, 1)]
                                     for n in ("run_arrived", "self_arrived"))
        rows_arrived, weighted_ready = ([[sem(f"{n}{l}_{k}") for k in range(PARTS)] for l in (0, 1)]
                                        for n in ("rows_arrived", "weighted_ready"))
        (staged, ids_ready, ids_staged, runs_taken, degree_now, more_arrived, more_ready, masked, logit_steps,
         shifted_ready, probs_ready, summed, acc_moved, block_kept) = (
            layered(n) for n in ("staged", "ids_ready", "ids_staged", "runs_taken", "degree_now", "more_arrived",
                                 "more_ready", "masked", "logit_steps", "shifted_ready", "probs_ready", "summed",
                                 "acc_moved", "block_kept"))
        dense_chain, variance_ready, root_ready, normed, norm_turned, norm_copied = (
            sem(n) for n in ("dense_chain", "variance_ready", "root_ready", "normed", "norm_turned", "norm_copied"))
        b_staged, b_qkv, b_rows = (sem(n) for n in ("b_staged", "b_qkv", "b_rows"))
        b_x, b_stored = pair("b_x"), pair("b_stored")
        c_staged, c_proj, c_gelu, c_up, c_down, c_out = (
            sem(n) for n in ("c_staged", "c_proj", "c_gelu", "c_up", "c_down", "c_out"))
        c_x, c_stored = pair("c_x"), pair("c_stored")

        LAYERS = [dict(H=H0, W=W0, vc=0, dv=65, rec=1, runs=neighbours, own=table[0][0:N, :], ownw=W0),
                  dict(H=H1, W=W1, vc=256, dv=33, rec=REC, runs=records[0:P * LANE + SLOTS, :], own=own1, ownw=2 * D)]

        def slots(l, k, n=R + 1):
            w = LAYERS[l]["W"]
            return V[k][:, 0:(R + 1) * w].rearrange("p (s w) -> p s w", w=w)[:, 0:n, :]

        def acc(l, k):
            c = LAYERS[l]
            return slots(l, k)[:, R, c["vc"]:c["vc"] + c["H"] * c["dv"]]

        PAIRS = GROUPS * GROUP // 2
        SCATTERED = 16 * GROUP * (GROUPS // 2)

        def prepared(h):
            return GROUPS // 2 + 1 - h
        group_recs = [runs[h][:, 0:GROUP * REC].rearrange("p (t c) -> p t c", c=REC) for h in range(2)]

        histp, smallp = bank[0], bank[1]
        degp = bank[0]
        countp = bank[2]
        turnp = [bank[3], bank[4]]
        lookp = [bank[5], bank[6]]
        keyrowp = [bank[7], bank[0]]

        block = ctx.enter_context(nc.Block())

        @block.sync
        def _(sp):
            sp.wait_ge(keys_padded, 1)
            for l, key in ((0, src), (1, dst)):
                sp.dma_start(keyi[l][0:P - 1, 0:LANE],
                             key[0:(P - 1) * LANE].rearrange("(p t) -> p t", t=LANE)).then_inc(keys_loaded[l], 16)
                sp.dma_start(keyi[l][P - 1:P, 0:LASTLANE],
                             key[(P - 1) * LANE:E].rearrange("(p t) -> p t", p=1)).then_inc(keys_loaded[l], 16)
            with nc.allow_non_contiguous_dma(reason="one edge of every partition"):
                sp.dma_start(lane_end[0:P - 2, :], dst[LANE:(P - 1) * LANE].rearrange("(p t) -> p t", t=LANE)[:, 0:1])\
                    .then_inc(keys_loaded[1], 16)
                sp.dma_start(lane_end[P - 2:P - 1, :], dst[(P - 1) * LANE:(P - 1) * LANE + 1].rearrange("(p t) -> p t", t=1))\
                    .then_inc(keys_loaded[1], 16)
            sp.dma_start(neighbours[E:E + SLOTS, :].rearrange("a b -> b a"), zrow[:, :]).then_inc(pad_written, 16)
            sp.dma_start(records[P * LANE:P * LANE + SLOTS, :].rearrange("(o a) b -> o (a b)", o=1),
                         zrec[:, :]).then_inc(recpad_written, 16)
            sp.dma_start(a_all[:, :, :], a.rearrange("(u h) o -> u h o", u=1).broadcast_to([P, 4, P])).then_inc(weights_loaded, 16)
            for c in range(2):
                rows = slice(c * P, (c + 1) * P)
                sp.dma_start(wext[:, c, 0:D].rearrange("p (h o) -> p h o", h=4),
                             W[:, rows, :].rearrange("h p o -> p h o")).then_inc(weights_loaded, 16)
                sp.dma_start(qkv_sb[:, c, :], qkv_w[rows, :]).then_inc(weights_loaded, 16)
                sp.dma_start(in_sb[:, c, :], in_w[rows, :]).then_inc(weights_loaded, 16)
                sp.dma_start(f1_sb[:, c, :], f1_w[rows, :]).then_inc(weights_loaded, 16)
            sp.dma_start(f2_sb[:, :, :], f2_w.rearrange("(c p) n -> p c n", p=P)).then_inc(weights_loaded, 16)
            for tile, vec in ((qkv_bias, qkv_b), (in_bias, in_b), (f2_bias, f2_b)):
                sp.dma_start(tile[:, :], vec.rearrange("(u n) -> u n", u=1).broadcast_to([P, vec.shape[0]])).then_inc(weights_loaded, 16)
            with nc.allow_non_contiguous_dma(reason="one small vector by column"):
                sp.dma_start(f1_bias[:, :], f1_b.rearrange("(c p) -> p c", p=P)).then_inc(weights_loaded, 16)
                for n, vec in enumerate((ln1_g, ln1_b, res_g, res_b)):
                    sp.dma_start(lncol[:, n, :], vec.rearrange("(c p) -> p c", p=P)).then_inc(weights_loaded, 16)

            def load_order(l):
                sp.wait_ge(order_written[l], 16 * BLOCKS)
                sp.dma_start(bt[l][:, 0:BLOCKS, :], order[l].rearrange("(b p) c -> p b c", p=P)).then_inc(order_loaded[l], 16)

            def load_x(row, h):
                sp.dma_start(xt[h][:, :], x[bass.ds(row, P), :]).then_inc(x_loaded[h], 16)

            def store_rows(row, h, n):
                sp.wait_ge(hrow_ready[h], n + 1)
                sp.dma_start(table[0][bass.ds(row, P), :], hrow[h][:, :]).then_inc(hrow_stored[h], 16)
            load_x(0, 0)
            load_x(P, 1)
            with sp.Fori(0, (HI - 1) // 2 - 1) as it:
                for h in range(2):
                    row = it * (2 * P) + h * P
                    store_rows(row, h, it)
                    load_x(row + 2 * P, h)
            store_rows((HI - 3) * P, 0, (HI - 1) // 2 - 1)
            load_x(N - P, 0)
            store_rows((HI - 2) * P, 1, (HI - 1) // 2 - 1)
            sp.wait_ge(hrow_stored[1], 16 * ((HI - 1) // 2))
            store_rows(N - P, 0, (HI - 1) // 2)
            sp.wait_ge(hrow_stored[0], 16 * ((HI + 1) // 2))
            load_order(0)
            for c, (t, n) in enumerate(rec_tiles):
                h = c % 2
                lanes = P if t + n <= LASTLANE else P - 1
                if c >= 2:
                    sp.wait_ge(recs_ready[h], c // 2)
                for tile, attr in ((attr1, attr_a), (attr2, attr_b)):
                    sp.dma_start(tile[h][0:P - 1, 0:n, :], attr[0:(P - 1) * LANE, :].rearrange(
                        "(p t) c -> p t c", t=LANE)[:, t:t + n, :]).then_inc(attrs_loaded[h], 16)
                    m = max(1, min(n, LASTLANE - t))
                    t_last = min(t, LASTLANE - 1)
                    sp.dma_start(tile[h][P - 1:P, 0:m, :], attr[(P - 1) * LANE:E, :].rearrange(
                        "(p t) c -> p t c", p=1)[:, t_last:t_last + m, :]).then_inc(attrs_loaded[h], 16)
                sp.wait_ge(recs_ready[h], c // 2 + 1)
                sp.dma_start(records[0:P * LANE, :].rearrange("(p t) c -> p t c", t=LANE)[:, t:t + n, :],
                             recs[h][:, 0:n, :]).then_inc(recs_stored[h], 16)
            for h in range(2):
                sp.wait_ge(recs_stored[h], 64)
            sp.wait_ge(recpad_written, 16)
            load_order(1)
            sp.wait_ge(order_loaded[0], 16)
            sp.wait_ge(order_loaded[1], 16)
            sp.wait_ge(pad_written, 16)
            sp.wait_ge(meta_ready[1], 1)
            with sp.If(sp.value_load(unsorted[0:1, 0:1], min_val=0, max_val=1)):
                with sp.Fori(0, GROUPS // 2) as it:
                    for h in range(2):
                        with sp.If(it):
                            sp.wait_ge(scattered[h], it * (16 * GROUP) + SCATTERED)
                            sp.sem_inc(waits_done, 1)
                        t0 = it * (2 * GROUP) + h * GROUP
                        sp.dma_start(group_recs[h], records[bass.ds(t0, P * LANE), :].rearrange(
                            "(p t) c -> p t c", t=LANE)[:, 0:GROUP, :]).then_inc(group_loaded[h], 16)
                for h in range(2):
                    sp.wait_ge(scattered[h], 2 * SCATTERED)
                sp.dma_start(records[0:E, :].rearrange("(a p) c -> a (p c)", a=125),
                             resorted.rearrange("(a p) c -> a (p c)", a=125)).then_inc(resorted_moved, 16)
                sp.wait_ge(resorted_moved, 16)

        @block.gpsimd
        def _(pool):
            pool.iota(counti[:, :], pattern=[[1, P]], base=0, channel_multiplier=0)
            pool.iota(nodei[:, :], pattern=[[P, BLOCKS]], base=0, channel_multiplier=1).then_inc(iotas_ready, 1)
            pool.memset(identf[:, :], 0.0)
            pool.memset(before[:, :], 1.0)
            pool.memset(earlier[:, :], 1.0).then_inc(masks_ready, 1)
            pool.wait_ge(masks_ready, 1)
            pool.affine_select(out=identf[:, :], in_=identf[:, :], compare_op=ALU.not_equal, fill=1.0,
                               base=0, pattern=[[-1, P]], channel_multiplier=1)
            pool.affine_select(out=before[:, :], in_=before[:, :], compare_op=ALU.is_gt, fill=0.0,
                               base=0, pattern=[[1, P]], channel_multiplier=-1)
            pool.affine_select(out=earlier[:, P:2 * P], in_=earlier[:, P:2 * P], compare_op=ALU.is_gt, fill=0.0,
                               base=0, pattern=[[-1, P]], channel_multiplier=1).then_inc(masks_ready, 1)

            def write_order(l):
                pool.wait_ge(places_ready, l + 1)
                for b in range(BLOCKS):
                    pool.indirect_dma_start(
                        out=order[l], out_offset=bass.IndirectOffsetOnAxis(ap=placei[l][:, b:b + 1], axis=0),
                        in_=rec[l][:, b, :], in_offset=None).then_inc(order_written[l], 16)

            def scatter_edges(l):
                last_place = pool.to_reg(E - 1)
                with pool.Fori(0, GROUPS // 2) as it:
                    for h in range(2):
                        pool.wait_ge(targets_ready[h], it + (1 + l * (GROUPS // 2)))
                        pool.sem_inc(waits_done, 1)
                        if l:
                            pool.wait_ge(group_loaded[h], it * 16 + 16)
                            pool.sem_inc(waits_done, 1)
                        for j in range(GROUP):
                            pool.indirect_dma_start(
                                out=(neighbours, resorted)[l], out_offset=bass.IndirectOffsetOnAxis(ap=target[h][:, j:j + 1], axis=0),
                                in_=group_recs[h][:, j, :] if l else payload[h][:, j:j + 1], in_offset=None,
                                bounds_check=last_place, oob_is_err=False).then_inc(scattered[h], 16)

            def arrived(s, v):
                pool.wait_ge(s, v)
                pool.sem_inc(waits_done, 1)

            def aggregate(l):
                c = LAYERS[l]
                last_row = None

                def run_of(at, to, s):
                    pool.indirect_dma_start(
                        out=to[:, 0:SLOTS * c["rec"]], out_offset=None,
                        in_=c["runs"].rearrange("(o a) b -> o a b", o=1),
                        in_offset=bass.IndirectOffsetOnAxis(ap=at[:, 0:1], axis=1)).then_inc(s, 16)

                def begin(b, h, n):
                    pool.tensor_copy(first_at[h][:, :], bt[l][:, bass.ds(b, 1), 1])
                    pool.tensor_copy(node_at[h][:, :], bt[l][:, bass.ds(b, 1), 3]).then_inc(staged[l], 1)
                    arrived(staged[l], n)
                    run_of(first_at[h], runs[h], run_arrived[l][h])
                    pool.indirect_dma_start(
                        out=self_rows[h][:, 0:c["ownw"]], out_offset=None, in_=c["own"],
                        in_offset=bass.IndirectOffsetOnAxis(ap=node_at[h][:, 0:1], axis=0)).then_inc(self_arrived[l][h], 16)

                pool.wait_ge(meta_ready[l], 1)
                begin(0, 0, 1)
                with pool.Fori(0, BLOCKS // 2) as b2:
                    for h in range(2):
                        b = b2 * 2 + h
                        steps = pool.value_load(meta[l][0:1, 0, bass.ds(b, 1)], min_val=1, max_val=E)
                        done = pool.value_load(meta[l][0:1, 1, bass.ds(b, 1)], min_val=0, max_val=E)
                        runs_done = pool.value_load(meta[l][0:1, 2, bass.ds(b, 1)], min_val=0, max_val=E)
                        arrived(runs_taken[l], b + runs_done + 1)
                        begin(b + 1, 1 - h, b + 2)
                        arrived(run_arrived[l][h], b2 * 16 + 16)
                        pool.tensor_copy(firstf[:, :], bt[l][:, bass.ds(b, 1), 1])
                        pool.tensor_copy(ids[:, :], runs[h][:, 0:SLOTS * c["rec"]].rearrange(
                            "p (s c) -> p s c", c=c["rec"])[:, :, 0]).then_inc(ids_ready[l], 1)
                        arrived(ids_ready[l], b + runs_done + 1)
                        with pool.Fori(0, steps) as i:
                            g = pool.snap(done + i)
                            for k in range(PARTS):
                                arrived(weighted_ready[l][k], g + 1)
                                pool.tensor_copy(ids_part[k][:, :], ids[:, bass.ds((i & 3) * G + k * R, R)])\
                                    .then_inc(ids_staged[l], 1)
                                arrived(ids_staged[l], g * PARTS + (k + 1))
                                for r in range(R):
                                    pool.indirect_dma_start(
                                        out=slots(l, k)[:, r, :], out_offset=None, in_=table[l][0:(N, ROWS)[l], :],
                                        in_offset=bass.IndirectOffsetOnAxis(ap=ids_part[k][:, r:r + 1], axis=0))\
                                        .then_inc(rows_arrived[l][k], 16)
                            with pool.If(((i & 3) + 1) >> 2):
                                n = runs_done + (i >> 2)
                                arrived(runs_taken[l], b + n + 2)
                                pool.tensor_scalar(firstf[:, :], firstf[:, :], float(SLOTS), float(E), ALU.add, ALU.min)\
                                    .then_inc(more_ready[l], 1)
                                arrived(more_ready[l], n * 2 + 1)
                                pool.tensor_copy(more_at[:, :], firstf[:, :]).then_inc(more_ready[l], 1)
                                arrived(more_ready[l], n * 2 + 2)
                                run_of(more_at, more, more_arrived[l])
                                arrived(more_arrived[l], n * 16 + 16)
                                pool.tensor_copy(ids[:, :], more[:, 0:SLOTS * c["rec"]].rearrange(
                                    "p (s c) -> p s c", c=c["rec"])[:, :, 0]).then_inc(ids_ready[l], 1)
                                arrived(ids_ready[l], b + n + 2)
                pool.wait_ge(run_arrived[l][0], 16 * (BLOCKS // 2 + 1))
                pool.wait_ge(self_arrived[l][0], 16 * (BLOCKS // 2 + 1))

            def gather(to, tab, at, s):
                pool.indirect_dma_start(out=to, out_offset=None, in_=tab,
                                        in_offset=bass.IndirectOffsetOnAxis(ap=at[:, 0:1], axis=0)).then_inc(s, 16)

            def scatter(tab, at, what, s, bound=None):
                extra = {} if bound is None else dict(bounds_check=bound, oob_is_err=False)
                pool.indirect_dma_start(out=tab, out_offset=bass.IndirectOffsetOnAxis(ap=at[:, 0:1], axis=0),
                                        in_=what, in_offset=None, **extra).then_inc(s, 16)

            def dense_b():
                def begin(b, h, n):
                    pool.tensor_copy(node_at[h][:, :], bt[0][:, bass.ds(b, 1), 3])
                    pool.tensor_copy(raw_at[h][:, :], bt[0][:, bass.ds(b, 1), 0]).then_inc(b_staged, 1)
                    arrived(b_staged, n)
                    gather(xg[h][:, 0:D], x, node_at[h], b_x[h])
                begin(0, 0, 1)
                with pool.Fori(0, BLOCKS // 2) as b2:
                    for h in range(2):
                        b = b2 * 2 + h
                        with pool.If(b):
                            arrived(b_stored[1 - h], b2 * 32 + 32 * h)
                        begin(b + 1, 1 - h, b + 2)
                        arrived(b_rows, b + 1)
                        scatter(table[1], raw_at[h], qv[h][:, :], b_stored[h])
                        scatter(own1, raw_at[h], kx[h][:, :], b_stored[h])
                for h in range(2):
                    pool.wait_ge(b_stored[h], 16 * BLOCKS)
                pool.wait_ge(b_x[0], 16 * (BLOCKS // 2 + 1))

            def dense_c():
                last_node = pool.to_reg(N - 1)

                def begin(b, h, n):
                    pool.tensor_copy(node_at[h][:, :], bt[1][:, bass.ds(b, 1), 3])
                    pool.tensor_copy(raw_at[h][:, :], bt[1][:, bass.ds(b, 1), 0]).then_inc(c_staged, 1)
                    arrived(c_staged, n)
                    gather(xg[h][:, :], own1, node_at[h], c_x[h])
                begin(0, 0, 1)
                with pool.Fori(0, BLOCKS // 2) as b2:
                    for h in range(2):
                        b = b2 * 2 + h
                        with pool.If(b):
                            arrived(c_stored[1 - h], b2 * 16 + 16 * h)
                        begin(b + 1, 1 - h, b + 2)
                        arrived(c_out, b + 1)
                        scatter(out, raw_at[h], outrow[h][:, :], c_stored[h], last_node)
                for h in range(2):
                    pool.wait_ge(c_stored[h], 16 * (BLOCKS // 2))
                pool.wait_ge(c_x[0], 16 * (BLOCKS // 2 + 1))

            write_order(0)
            scatter_edges(0)
            write_order(1)
            for h in range(2):
                pool.wait_ge(scattered[h], SCATTERED)
            pool.wait_ge(meta_ready[1], 1)
            with pool.If(pool.value_load(unsorted[0:1, 0:1], min_val=0, max_val=1)):
                scatter_edges(1)
                pool.wait_ge(resorted_moved, 16)
                pool.sem_inc(waits_done, 1)
            for h in range(2):
                pool.wait_ge(hrow_stored[h], 16 * ((HI - 1) // 2 + (1 - h)))
            pool.wait_ge(pad_written, 16)
            aggregate(0)
            dense_b()
            for h in range(2):
                pool.wait_ge(recs_stored[h], 64)
            pool.wait_ge(recpad_written, 16)
            aggregate(1)
            dense_c()

        @block.scalar
        def _(act):
            def rank_edges(l):
                def prepare(h, n):
                    act.wait_ge(turned[h], n + 1 + l * prepared(h))
                    nc.scalar.copy(oneAT[h][:, :], turnp[h][0:HI, :].bitcast(bf16)[:, 0:GROUP * P]).then_inc(turned_copied[h], 1)
                prepare(0, 0)
                with act.Fori(0, GROUPS // 2) as it:
                    for h in range(2):
                        for pair_ in range(GROUP // 2):
                            n = it * GROUP + (GROUP // 2 * h + pair_)
                            act.wait_ge(count_ready, n + 1 + l * (PAIRS + 1))
                            nc.scalar.copy(count[pair_][:, :], countp[0:HI, 0:P]).then_inc(count_copied, 1)
                        prepare(1 - h, it + h)

            def rows_before():
                def one(h, n):
                    act.wait_ge(x_turned[h], n + 1)
                    nc.scalar.copy(xT[h][:, :, :].rearrange("p c n -> p (c n)"), bank[3 + h][:, 0:D]).then_inc(xT_copied[h], 1)
                with act.Fori(0, (HI - 1) // 2) as it:
                    for h in range(2):
                        one(h, it)
                one(0, (HI - 1) // 2)

            def aggregate(l):
                c = LAYERS[l]
                w, hs = c["H"] * c["dv"], (R + 1) * c["H"]
                act.wait_ge(meta_ready[l], 1)
                with act.Fori(0, BLOCKS) as b:
                    steps = act.value_load(meta[l][0:1, 0, bass.ds(b, 1)], min_val=1, max_val=E)
                    done = act.value_load(meta[l][0:1, 1, bass.ds(b, 1)], min_val=0, max_val=E)
                    with act.Fori(0, steps) as i:
                        g = act.snap((done + i) * PARTS)
                        for k in range(PARTS):
                            q = act.snap(g + (k + 1))
                            act.wait_ge(shifted_ready[l], q)
                            nc.scalar.activation(probs[k][:, 0:hs], shifted[k][:, 0:hs], ACT.Exp).then_inc(probs_ready[l], 1)
                            act.wait_ge(summed[l], q)
                            nc.scalar.copy(acc(l, (k + 1) % PARTS), bank[5 + k][:, 0:w]).then_inc(acc_moved[l], 1)
                    act.wait_ge(acc_moved[l], (done + steps) * PARTS + 1)
                    nc.scalar.copy(sums[:, b, 0:w], acc(l, 0)).then_inc(block_kept[l], 1)

            def affine_turned(ln, done, turned_sem, copied_sem):
                act.wait_ge(turned_sem, done + 1)
                for half in range(2):
                    last = nc.scalar.activation(tT[:, half, :], bank[3][:, half * P:(half + 1) * P], ACT.Identity,
                                                bias=lncol[:, 2 * ln + 1, half:half + 1], scale=lncol[:, 2 * ln, half:half + 1])
                last.then_inc(copied_sem, 1)

            def root(n, done, var_sem, std_sem):
                act.wait_ge(var_sem, done + 1)
                nc.scalar.activation(std[:, n, 0:1], mv[:, n, 1:2], ACT.Sqrt, bias=eps_sb[:, :]).then_inc(std_sem, 1)

            def dense_b():
                with act.Fori(0, BLOCKS) as b:
                    root(0, b * 2, variance_ready, root_ready)
                    root(1, b * 2 + 1, variance_ready, root_ready)
                    affine_turned(0, b, norm_turned, norm_copied)

            def dense_c():
                with act.Fori(0, BLOCKS) as b:
                    act.wait_ge(norm_turned, b * 2 + (BLOCKS + 1))
                    nc.scalar.copy(tT[:, :, :].rearrange("p c n -> p (c n)"), bank[3][:, 0:D]).then_inc(norm_copied, 1)
                    root(0, b * 2 + 2 * BLOCKS, variance_ready, root_ready)
                    affine_turned(1, b * 2 + (BLOCKS + 1), norm_turned, norm_copied)
                    act.wait_ge(c_up, b + 1)
                    for j in range(8):
                        last = nc.scalar.activation(gT[:, j, :], bank[5 + j // 4][:, (j % 4) * P:(j % 4 + 1) * P],
                                                    ACT.Gelu, bias=f1_bias[:, j:j + 1])
                    last.then_inc(c_gelu, 1)
                    root(1, b * 2 + (2 * BLOCKS + 1), variance_ready, root_ready)

            act.wait_ge(weights_loaded, 16 * 18)
            rows_before()
            rank_edges(0)
            act.wait_ge(meta_ready[1], 1)
            with act.If(act.value_load(unsorted[0:1, 0:1], min_val=0, max_val=1)):
                rank_edges(1)
            aggregate(0)
            dense_b()
            aggregate(1)
            dense_c()

        @block.tensor
        def _(pe):
            def histogram(l):
                nc.tensor.matmul(histp[0:HI, 0:P], zerob[:, 0:HI], zerob[:, :], start=True, stop=False)
                with pe.Fori(0, TILES // HB // 2) as it:
                    for h in range(2):
                        pe.wait_ge(hist_onehots[h], it + 1 + l * (TILES // HB // 2))
                        for j in range(HB):
                            last = nc.tensor.matmul(histp[0:HI, 0:P], hA[h][:, j, :], hB[h][:, j, :],
                                                    start=False, stop=False)
                        last.then_inc(hist_taken[h], 1)
                nc.tensor.matmul(histp[0:HI, 0:P], zerob[:, 0:HI], zerob[:, :], start=False, stop=True).then_inc(hist_done, 1)

            def offsets(l):
                pe.wait_ge(totals_ready, l + 1)
                nc.tensor.matmul(smallp[0:1, 1:2], drops[:, :], ones128[:, 0:1], start=True, stop=True)
                nc.tensor.matmul(smallp[0:HI, 0:1], before[0:HI, 0:HI], upto[:, P - 1:P],
                                 start=True, stop=True).then_inc(base_ready, 1)
                pe.wait_ge(tables_ready, l + 1)
                nc.tensor.transpose(smallp[:, 128:128 + HI], degree[:, :], identf[0:HI, 0:HI])
                nc.tensor.transpose(smallp[:, 256:256 + HI], firsts[l][:, :], identf[0:HI, 0:HI]).then_inc(tables_turned, 1)

            def sort_by_degree(l):
                pe.wait_ge(deg_onehots, l + 1)
                with pe.Fori(0, BLOCKS - 1) as b:
                    nc.tensor.matmul(degp[:, 0:P], onesb[:, :], degone[:, b, :], start=False, stop=False)
                nc.tensor.matmul(degp[:, 0:P], onesb[:, :], degone[:, BLOCKS - 1, :],
                                 start=False, stop=True).then_inc(deg_hist, 1)
                pe.wait_ge(degbase_ready, l + 1)
                nc.tensor.matmul(degp[:, 0:P], identf[:, :], degbase[:, :], start=True, stop=True, skip_group_check=True)
                with pe.Fori(0, BLOCKS) as b:
                    nc.tensor.matmul(degp[:, 0:P], beforeb[:, :], degone[:, b, :],
                                     start=False, stop=True, skip_group_check=True).then_inc(degsum_ready, 1)
                    pe.wait_ge(degplace_ready, b + (1 + l * BLOCKS))
                    nc.tensor.matmul(degp[:, 0:P], notbeforeb[:, :], degone[:, b, :],
                                     start=False, stop=True, skip_group_check=True)
                pe.wait_ge(order_loaded[l], 16)
                nc.tensor.transpose(smallp[0:BLOCKS, 384:512], bt[l][:, 0:BLOCKS, 2], identf[:, :]).then_inc(turned_degree, 1)
                pe.wait_ge(blockmax_ready, l + 1)
                nc.tensor.matmul(smallp[0:1, 64:64 + BLOCKS], blockmax[:, :], identf[0:BLOCKS, 0:BLOCKS],
                                 start=True, stop=True).then_inc(maxrow_ready, 1)

            def rank_edges(l):
                if l:
                    pe.wait_ge(turned_copied[0], prepared(0))
                    pe.wait_ge(turned_copied[1], prepared(1))
                nc.tensor.matmul(countp[0:HI, 0:P], identf[0:HI, 0:HI], firsts[l][:, :],
                                 start=True, stop=True, skip_group_check=True).then_inc(count_ready, 1)

                def prepare(h, n):
                    pe.wait_ge(onehots_ready[h], n + 1 + l * prepared(h))
                    for j in range(GROUP):
                        for half in range(2):
                            last = nc.tensor.matmul(
                                keyrowp[h][:, j * P:(j + 1) * P],
                                keycol[h][:, half, j:j + 1].to_broadcast([P, P]), identb[:, :],
                                start=half == 0, stop=half == 1)
                    last.then_inc(keyrows_ready[h], 1)
                    for j in range(GROUP):
                        last = nc.tensor.transpose(turnp[h][0:HI, :].bitcast(bf16)[:, j * P:(j + 1) * P],
                                                   oneA[h][:, j, :], identb[:, :])
                    last.then_inc(turned[h], 1)
                prepare(0, 0)
                with pe.Fori(0, GROUPS // 2) as it:
                    for h in range(2):
                        pe.wait_ge(turned_copied[h], it + 1 + l * prepared(h))
                        for pair_ in range(GROUP // 2):
                            pe.wait_ge(count_copied, it * GROUP + (GROUP // 2 * h + pair_ + 1 + l * PAIRS))
                            for j in (2 * pair_, 2 * pair_ + 1):
                                last = nc.tensor.matmul(lookp[h][:, j * P:(j + 1) * P], oneAT[h][:, j * P:(j + 1) * P],
                                                        count[pair_][:, :], start=True, stop=True)
                            if pair_:
                                last.then_inc(lookup_ready, 1)
                            for j in (2 * pair_, 2 * pair_ + 1):
                                last = nc.tensor.matmul(countp[0:HI, 0:P], oneA[h][:, j, :], oneB[h][:, j, :],
                                                        start=False, stop=True, skip_group_check=True)
                            last.then_inc(count_ready, 1)
                            if pair_ == 0:
                                prepare(1 - h, it + h)

            def rows_before():
                def one(h, n):
                    pe.wait_ge(x_loaded[h], n * 16 + 16)
                    pe.wait_ge(xT_copied[h], n + 1)
                    for half in range(2):
                        last = nc.tensor.transpose(bank[3 + h][:, half * P:(half + 1) * P],
                                                   xt[h][:, half * P:(half + 1) * P], identf[:, :])
                    last.then_inc(x_turned[h], 1)
                    pe.wait_ge(xT_copied[h], n + 2)
                    pe.wait_ge(h_moved[h], n + 1)
                    for half in range(2):
                        last = nc.tensor.matmul(bank[5 + h][:, 0:264], xT[h][:, half, :], wext[:, half, :],
                                                start=half == 0, stop=half == 1)
                    last.then_inc(h_ready[h], 1)
                pe.wait_ge(wext_ready, 1)
                with pe.Fori(0, (HI - 1) // 2) as it:
                    for h in range(2):
                        one(h, it)
                one(0, (HI - 1) // 2)

            def aggregate(l):
                c = LAYERS[l]
                w = c["H"] * c["dv"]
                pe.wait_ge(meta_ready[l], 1)
                with pe.Fori(0, BLOCKS) as b:
                    steps = pe.value_load(meta[l][0:1, 0, bass.ds(b, 1)], min_val=1, max_val=E)
                    done = pe.value_load(meta[l][0:1, 1, bass.ds(b, 1)], min_val=0, max_val=E)
                    with pe.Fori(0, steps) as i:
                        g = pe.snap(done + i + 2)
                        for k in range(PARTS):
                            pe.wait_ge(weighted_ready[l][k], g)
                            for r in range(R + 1):
                                last = nc.tensor.matmul(bank[5 + k][:, 0:w], identf[:, :], weighted[k][:, r, 0:w],
                                                        start=r == 0, stop=r == R)
                            last.then_inc(summed[l], 1)

            def turn(what, s):
                for half in range(2):
                    last = nc.tensor.transpose(bank[3][:, half * P:(half + 1) * P], what[:, half * P:(half + 1) * P], identf[:, :])
                last.then_inc(s, 1)

            def dense_b():
                with pe.Fori(0, BLOCKS) as b:
                    pe.wait_ge(normed, b + 1)
                    turn(zn, norm_turned)
                    pe.wait_ge(norm_copied, b + 1)
                    for to, cols in ((bank[5], slice(0, 512)), (bank[6], slice(512, 768))):
                        for half in range(2):
                            last = nc.tensor.matmul(to[:, 0:cols.stop - cols.start], tT[:, half, :], qkv_sb[:, half, cols],
                                                    start=half == 0, stop=half == 1)
                    last.then_inc(b_qkv, 1)

            def dense_c():
                with pe.Fori(0, BLOCKS) as b:
                    pe.wait_ge(normed, b * 2 + (BLOCKS + 1))
                    turn(aggn, norm_turned)
                    pe.wait_ge(norm_copied, b * 2 + (BLOCKS + 1))
                    for half in range(2):
                        last = nc.tensor.matmul(bank[4][:, 0:D], tT[:, half, :], in_sb[:, half, :],
                                                start=half == 0, stop=half == 1)
                    last.then_inc(c_proj, 1)
                    pe.wait_ge(normed, b * 2 + (BLOCKS + 2))
                    turn(zn, norm_turned)
                    pe.wait_ge(norm_copied, b * 2 + (BLOCKS + 2))
                    for j in range(8):
                        for half in range(2):
                            last = nc.tensor.matmul(bank[5 + j // 4][:, (j % 4) * P:(j % 4 + 1) * P],
                                                    f1_sb[:, half, j * P:(j + 1) * P], tT[:, half, :],
                                                    start=half == 0, stop=half == 1)
                    last.then_inc(c_up, 1)
                    pe.wait_ge(c_gelu, b + 1)
                    for j in range(8):
                        last = nc.tensor.matmul(bank[7][:, 0:D], gT[:, j, :], f2_sb[:, j, :], start=j == 0, stop=j == 7)
                    last.then_inc(c_down, 1)

            pe.wait_ge(consts_ready, 1)
            rows_before()
            histogram(0)
            offsets(0)
            nc.tensor.matmul(degp[:, 0:P], zerob[:, :], zerob[:, :], start=True, stop=False)
            sort_by_degree(0)
            rank_edges(0)
            pe.wait_ge(looked_up, GROUPS)
            histogram(1)
            offsets(1)
            nc.tensor.matmul(degp[:, 0:P], zerob[:, :], zerob[:, :], start=True, stop=False)
            sort_by_degree(1)
            pe.wait_ge(meta_ready[1], 1)
            with pe.If(pe.value_load(unsorted[0:1, 0:1], min_val=0, max_val=1)):
                rank_edges(1)
            aggregate(0)
            dense_b()
            aggregate(1)
            dense_c()

        @block.vector
        def _(dve):
            chained = [0]

            def link(ins):
                chained[0] += 1
                ins.then_inc(setup_chain, 1)
                dve.wait_ge(setup_chain, chained[0])

            dve.memset(keyi[0][:, :], PADKEY)
            dve.memset(keyi[1][:, :], PADKEY)
            dve.memset(lane_end[:, :], PADKEY)
            dve.memset(zrec[:, :], 0.0)
            for l in (0, 1):
                dve.memset(bt[l][:, BLOCKS, :], 0.0)
            dve.memset(eps_sb[:, :], EPS)
            for h in range(2):
                dve.memset(attr1[h][:, :, :], 0.0)
                dve.memset(attr2[h][:, :, :], 0.0)
                dve.memset(qv[h][:, :], 1.0)
            for k in range(PARTS):
                dve.memset(V[k][:, :], 0.0)
            dve.memset(zrow[:, :], 0.0).then_inc(keys_padded, 1)
            for h in range(2):
                for s in (hist_taken[h], xT_copied[h], h_moved[h]):
                    dve.sem_inc(s, 1)
            for l in (0, 1):
                for s in (runs_taken[l], *weighted_ready[l]):
                    dve.sem_inc(s, 1)
            dve.memset(zerob[:, :], 0.0)
            dve.memset(onesb[:, :], 1.0)
            dve.memset(ones128[:, :], 1.0)
            dve.wait_ge(iotas_ready, 1)
            nc.vector.tensor_copy(countf[:, :], counti[:, :])
            nc.vector.tensor_copy(countb[:, :], counti[:, :])
            for l in (0, 1):
                nc.vector.tensor_copy(rec[l][:, :, 0], nodei[:, :])
                nc.vector.tensor_scalar(rec[l][:, :, 3], nodei[:, :], float(N - 1), None, ALU.min)
            dve.wait_ge(masks_ready, 2)
            nc.vector.tensor_copy(identb[:, :], identf[:, :])
            nc.vector.tensor_copy(beforeb[:, :], before[:, :])
            nc.vector.tensor_scalar(notbeforeb[:, :], before[:, :], -1.0, 1.0, ALU.mult, ALU.add).then_inc(consts_ready, 1)
            dve.wait_ge(consts_ready, 1)
            for l in (0, 1):
                dve.wait_ge(keys_loaded[l], (32, 64)[l])
                nc.vector.tensor_copy(keyf[l][:, :], keyi[l][:, :])
                link(nc.vector.tensor_single_scalar(halfi[:, :], keyi[l][:, :], 7, ALU.arith_shift_right))
                link(nc.vector.tensor_copy(hib[l][:, :], halfi[:, :]))
                link(nc.vector.tensor_single_scalar(halfi[:, :], keyi[l][:, :], 127, ALU.bitwise_and))
                link(nc.vector.tensor_copy(lob[l][:, :], halfi[:, :]))
            link(nc.vector.scalar_tensor_tensor(padadd[:, 0:TILES], keyf[1][:, 0:TILES], 1.0, keyf[1][:, 1:TILES + 1],
                                                ALU.mult, ALU.is_gt, accum_out=drops[:, :]))
            link(nc.vector.tensor_tensor(dropped[:, :], keyf[1][:, LANE - 1:LANE], lane_end[:, :], ALU.is_gt))
            link(nc.vector.tensor_tensor(drops[:, :], drops[:, :], dropped[:, :], ALU.add))
            nc.vector.tensor_scalar(padadd[:, :], keyf[0][:, :], PADKEY - 0.5, OFF_TABLE, ALU.is_gt, ALU.mult).then_inc(halves_ready, 1)
            dve.wait_ge(halves_ready, 1)

            def onehots(hi_out, lo_out, l, t0, n):
                nc.vector.tensor_tensor(hi_out[:, :, :], hib[l][:, bass.ds(t0, n)].unsqueeze(2).to_broadcast([P, n, HI]),
                                        countb[:, 0:HI].unsqueeze(1).to_broadcast([P, n, HI]), ALU.is_equal)
                return nc.vector.tensor_tensor(lo_out[:, :, :], lob[l][:, bass.ds(t0, n)].unsqueeze(2).to_broadcast([P, n, P]),
                                               countb[:, :].unsqueeze(1).to_broadcast([P, n, P]), ALU.is_equal)

            def histogram(l):
                with dve.Fori(0, TILES // HB // 2) as it:
                    for h in range(2):
                        dve.wait_ge(hist_taken[h], it + 1 + l * (TILES // HB // 2))
                        onehots(hA[h], hB[h], l, it * (2 * HB) + h * HB, HB).then_inc(hist_onehots[h], 1)

            def offsets(l):
                dve.wait_ge(hist_done, l + 1)
                link(nc.vector.tensor_copy(degree[:, :], histp[0:HI, 0:P]))
                nc.vector.tensor_tensor_scan(upto[:, :], ones128[0:HI, :], degree[:, :], 0.0, ALU.mult, ALU.add).then_inc(totals_ready, 1)
                dve.wait_ge(totals_ready, l + 1)
                dve.wait_ge(base_ready, l + 1)
                nc.vector.tensor_scalar(unsorted[:, :], smallp[0:1, 1:2], 1.0, None, ALU.min)
                link(nc.vector.tensor_copy(blockbase[:, :], smallp[0:HI, 0:1]))
                nc.vector.scalar_tensor_tensor(firsts[l][:, :], upto[:, :], blockbase[:, 0:1], degree[:, :],
                                               ALU.add, ALU.subtract).then_inc(tables_ready, 1)
                dve.wait_ge(tables_turned, l + 1)
                nc.vector.memset(rec[l][:, :, 2], 0.0)
                nc.vector.memset(rec[l][:, :, 1], float(E))
                link(nc.vector.memset(degkey[:, :], 127.0))
                nc.vector.tensor_copy(rec[l][:, 0:HI, 2], smallp[:, 128:128 + HI])
                nc.vector.tensor_copy(rec[l][:, 0:HI, 1], smallp[:, 256:256 + HI])

            def sort_by_degree(l):
                link(nc.vector.tensor_scalar(degkey[:, 0:HI], smallp[:, 128:128 + HI], -1.0, 127.0, ALU.mult, ALU.add))
                link(nc.vector.tensor_scalar(degkeyb[:, :], degkey[:, :], 0.0, None, ALU.max))
                nc.vector.tensor_tensor(degone[:, :, :], degkeyb[:, :].unsqueeze(2).to_broadcast([P, BLOCKS, P]),
                                        countb[:, :].unsqueeze(1).to_broadcast([P, BLOCKS, P]), ALU.is_equal).then_inc(deg_onehots, 1)
                dve.wait_ge(deg_onehots, l + 1)
                dve.wait_ge(deg_hist, l + 1)
                link(nc.vector.tensor_copy(degbase[:, :], degp[:, 0:P]))
                link(nc.vector.tensor_tensor_scan(degincl[:, :], ones128[:, :], degbase[:, :], 0.0, ALU.mult, ALU.add))
                nc.vector.tensor_tensor(degbase[:, :], degincl[:, :], degbase[:, :], ALU.subtract).then_inc(degbase_ready, 1)
                dve.wait_ge(degbase_ready, l + 1)
                with dve.Fori(0, BLOCKS) as b:
                    dve.wait_ge(degsum_ready, b + (1 + l * BLOCKS))
                    nc.vector.scalar_tensor_tensor(junk[:, 0, 0:P], degone[:, b, :], 1.0, degp[:, 0:P], ALU.mult, ALU.mult,
                                                   accum_out=place[:, bass.ds(b, 1)]).then_inc(degplace_ready, 1)
                dve.wait_ge(degplace_ready, (l + 1) * BLOCKS)
                nc.vector.tensor_copy(placei[l][:, :], place[:, :]).then_inc(places_ready, 1)
                dve.wait_ge(turned_degree, l + 1)
                nc.vector.tensor_reduce(blockmax[:, :], smallp[0:BLOCKS, 384:512], AX, ALU.max).then_inc(blockmax_ready, 1)
                dve.wait_ge(maxrow_ready, l + 1)
                row = lambda r: mrow[:, r, :]
                link(nc.vector.tensor_scalar(row(0), smallp[0:1, 64:64 + BLOCKS], float(G - 1), float(DIV), ALU.add, ALU.mult))
                link(nc.vector.tensor_copy(mint[:, 0, :], row(0)))
                link(nc.vector.tensor_single_scalar(mint[:, 1, :], mint[:, 0, :], 16, ALU.arith_shift_right))
                link(nc.vector.tensor_scalar(row(0), mint[:, 1, :], 1.0, None, ALU.max))
                link(nc.vector.tensor_tensor_scan(row(1), ones128[0:1, 0:BLOCKS], row(0), 0.0, ALU.mult, ALU.add))
                nc.vector.tensor_copy(meta[l][:, 0, :], row(0))
                nc.vector.tensor_tensor(meta[l][:, 1, :], row(1), row(0), ALU.subtract)
                link(nc.vector.tensor_copy(mint[:, 0, :], row(0)))
                link(nc.vector.tensor_single_scalar(mint[:, 1, :], mint[:, 0, :], 2, ALU.arith_shift_right))
                link(nc.vector.tensor_copy(row(2), mint[:, 1, :]))
                link(nc.vector.tensor_tensor_scan(row(3), ones128[0:1, 0:BLOCKS], row(2), 0.0, ALU.mult, ALU.add))
                link(nc.vector.tensor_tensor(meta[l][:, 2, :], row(3), row(2), ALU.subtract))
                nc.vector.tensor_copy(meta[l][:, 0, :], row(0)).then_inc(meta_ready[l], 1)
                dve.wait_ge(meta_ready[l], 1)

            def rank_edges(l):
                def prepare(h, t0):
                    onehots(oneA[h], oneB[h], l, t0, GROUP)
                    nc.vector.tensor_scalar(keycol[h][:, 0, :], hib[l][:, bass.ds(t0, GROUP)], float(P), None, ALU.mult)
                    nc.vector.tensor_copy(keycol[h][:, 1, :], lob[l][:, bass.ds(t0, GROUP)]).then_inc(onehots_ready[h], 1)
                prepare(0, 0)
                with dve.Fori(0, GROUPS // 2) as it:
                    for h in range(2):
                        t0 = it * (2 * GROUP) + h * GROUP
                        dve.wait_ge(count_ready, it * GROUP + (GROUP // 2 * h + 1 + l * (PAIRS + 1)))
                        prepare(1 - h, t0 + GROUP)
                        dve.wait_ge(keyrows_ready[h], it + 1 + l * prepared(h))
                        for j in range(GROUP):
                            c0, n = (j - j % 2) * P, (j % 2 + 1) * P
                            last = nc.vector.scalar_tensor_tensor(
                                junk[:, GROUP * h + j, 0:n], keyrowp[h][:, c0:c0 + n], keyf[l][:, bass.ds(t0 + j, 1)],
                                earlier[:, P * (1 - j % 2):P * (1 - j % 2) + n],
                                ALU.is_equal, ALU.mult, accum_out=rank[h][:, j:j + 1])
                        with dve.If(it):
                            dve.wait_ge(scattered[h], it * (16 * GROUP) + l * SCATTERED)
                            dve.sem_inc(waits_done_dve, 1)
                        dve.wait_ge(lookup_ready, it * 2 + (h + 1 + l * GROUPS))
                        for j in range(GROUP):
                            last = nc.vector.scalar_tensor_tensor(
                                junk[:, GROUP * (2 + h) + j, 0:P], oneB[h][:, j, :], 1.0, lookp[h][:, j * P:(j + 1) * P],
                                ALU.mult, ALU.mult, accum_out=basis[h][:, j:j + 1])
                        last.then_inc(looked_up, 1)
                        if l == 0:
                            nc.vector.tensor_copy(payload[h][:, :], keyf[1][:, bass.ds(t0, GROUP)])
                        dve.wait_ge(looked_up, it * 2 + (h + 1 + l * GROUPS))
                        nc.vector.tensor_tensor(placef[h][:, :], basis[h][:, :], rank[h][:, :], ALU.add).then_inc(chain_rank, 1)
                        dve.wait_ge(chain_rank, it * 2 + (h + 1 + l * GROUPS))
                        nc.vector.tensor_tensor(target[h][:, :], placef[h][:, :], padadd[:, bass.ds(t0, GROUP)], ALU.add).then_inc(targets_ready[h], 1)

            def rows_before():
                dve.wait_ge(weights_loaded, 16 * 18)
                for half in range(2):
                    for cols, col in ((slice(64, 128), D), (slice(0, 64), D + 4)):
                        link(nc.vector.tensor_tensor(wprod[:, :, :], wext[:, half, 0:D].rearrange("p (h o) -> p h o", h=4),
                                                     a_all[:, :, cols], ALU.mult))
                        link(nc.vector.tensor_reduce(wext[:, half, col:col + 4], wprod[:, :, :], AX, ALU.add))
                nc.vector.tensor_scalar(qkv_bias[:, D:2 * D], qkv_bias[:, D:2 * D], 1.0 / 16, None, ALU.mult).then_inc(wext_ready, 1)
                dve.wait_ge(wext_ready, 1)

                def one(h, n):
                    dve.wait_ge(h_ready[h], n + 1)
                    nc.vector.tensor_copy(hrow[h][:, 0:260].rearrange("p (h o) -> p h o", h=4)[:, :, 0:64],
                                          bank[5 + h][:, 0:D].rearrange("p (h o) -> p h o", h=4))
                    nc.vector.tensor_copy(hrow[h][:, S2:S2 + 8], bank[5 + h][:, D:D + 8]).then_inc(hrow_ready[h], 1)
                    dve.wait_ge(hrow_ready[h], n + 1)
                    dve.sem_inc(h_moved[h], 1)
                one(0, 0)
                one(1, 0)
                with dve.Fori(1, (HI - 1) // 2) as it:
                    for h in range(2):
                        dve.wait_ge(hrow_stored[h], it * 16)
                        one(h, it)
                dve.wait_ge(hrow_stored[0], 16 * ((HI - 1) // 2))
                one(0, (HI - 1) // 2)
                for h in range(2):
                    dve.wait_ge(hrow_stored[h], 16 * ((HI - 1) // 2 + (1 - h)))
                    nc.vector.memset(qv[h][:, :], 1.0)

            def edge_records():
                for c, (t, n) in enumerate(rec_tiles):
                    h = c % 2
                    dve.wait_ge(attrs_loaded[h], 64 * (c // 2 + 1))
                    if c >= 2:
                        dve.wait_ge(recs_stored[h], 16 * (c // 2))
                    nc.vector.tensor_tensor(recs[h][:, 0:n, 1:REC], attr1[h][:, 0:n, :], attr2[h][:, 0:n, :], ALU.add)
                    nc.vector.tensor_copy(recs[h][:, 0:n, 0], keyf[0][:, t:t + n]).then_inc(recs_ready[h], 1)

            def aggregate(l):
                c = LAYERS[l]
                H, w = c["H"], c["H"] * c["dv"]

                def tile3(t, n=R + 1):
                    return t[:, 0:(R + 1) * H].rearrange("p (s h) -> p s h", h=H)[:, 0:n, :]

                def mask_run(run, n):
                    ins = nc.vector.tensor_scalar(mask[:, :], countf[:, 0:SLOTS], degnow[:, 0:1], LOWEST, ALU.is_ge, ALU.mult)
                    if l == 0:
                        ins.then_inc(runs_taken[l], 1)
                    else:
                        ins.then_inc(masked[l], 1)
                        dve.wait_ge(masked[l], n)
                        nc.vector.tensor_tensor(attrm[:, :, :], run[:, :].rearrange("p (s c) -> p s c", c=REC)[:, :, 1:REC],
                                                mask[:, :].unsqueeze(2).to_broadcast([P, SLOTS, 8]), ALU.add).then_inc(runs_taken[l], 1)

                with dve.Fori(0, BLOCKS // 2) as b2:
                    for h in range(2):
                        b = b2 * 2 + h
                        steps = dve.value_load(meta[l][0:1, 0, bass.ds(b, 1)], min_val=1, max_val=E)
                        done = dve.value_load(meta[l][0:1, 1, bass.ds(b, 1)], min_val=0, max_val=E)
                        runs_done = dve.value_load(meta[l][0:1, 2, bass.ds(b, 1)], min_val=0, max_val=E)
                        with dve.If(b):
                            dve.wait_ge(weighted_ready[l][PARTS - 1], done + 1)
                            dve.sem_inc(waits_done_dve, 1)
                        nc.vector.memset(tile3(logits[0])[:, R, :], LOWEST)
                        nc.vector.tensor_copy(degnow[:, :], bt[l][:, bass.ds(b, 1), 2]).then_inc(degree_now[l], 1)
                        dve.wait_ge(run_arrived[l][h], b2 * 16 + 16)
                        dve.wait_ge(self_arrived[l][h], b2 * 16 + 16)
                        if l == 0:
                            nc.vector.tensor_copy(own[:, 0:H], self_rows[h][:, S1:S1 + H])
                        else:
                            nc.vector.tensor_copy(own[:, :], self_rows[h][:, 0:D])
                        dve.wait_ge(degree_now[l], b + runs_done + 1)
                        mask_run(runs[h], b + runs_done + 1)
                        dve.wait_ge(runs_taken[l], b + runs_done + 2)
                        dve.sem_inc(waits_done_dve, 1)
                        with dve.Fori(0, steps) as i:
                            g = dve.snap(done + i)
                            for k in range(PARTS):
                                q = dve.snap(g * PARTS + (k + 1))
                                q4 = dve.snap(g * (4 * PARTS) + 4 * k)
                                nxt = (k + 1) % PARTS
                                dve.wait_ge(rows_arrived[l][k], g * (16 * R) + 16 * R)
                                lg = tile3(logits[k], R)
                                at = bass.ds((i & 3) * G + k * R, R)
                                if l == 0:
                                    t = tile3(qk, R)
                                    nc.vector.tensor_tensor(t, slots(l, k, R)[:, :, S2:S2 + H],
                                                            own[:, 0:H].unsqueeze(1).to_broadcast([P, R, H]), ALU.add)\
                                        .then_inc(logit_steps[l], 1)
                                    dve.wait_ge(logit_steps[l], q4 + 1)
                                    nc.vector.scalar_tensor_tensor(lg, t, 0.2, t, ALU.mult, ALU.max).then_inc(logit_steps[l], 1)
                                    add = mask[:, at].unsqueeze(2).to_broadcast([P, R, H])
                                else:
                                    nc.vector.tensor_tensor(qk[:, :].rearrange("p (r d) -> p r d", d=D), slots(l, k, R)[:, :, 0:D],
                                                            own[:, :].unsqueeze(1).to_broadcast([P, R, D]), ALU.mult)\
                                        .then_inc(logit_steps[l], 1)
                                    dve.wait_ge(logit_steps[l], q4 + 1)
                                    nc.vector.tensor_reduce(logits[k][:, 0:R * H], qk[:, :].rearrange("p (m d) -> p m d", d=32),
                                                            AX, ALU.add).then_inc(logit_steps[l], 1)
                                    add = attrm[:, at, :]
                                dve.wait_ge(logit_steps[l], q4 + 2)
                                nc.vector.tensor_tensor(lg, lg, add, ALU.add).then_inc(logit_steps[l], 1)
                                dve.wait_ge(logit_steps[l], q4 + 3)
                                top = tile3(logits[nxt])[:, R, :]
                                nc.vector.tensor_reduce(top, tile3(logits[k]).rearrange("p s h -> p h s"), AX, ALU.max)\
                                    .then_inc(logit_steps[l], 1)
                                dve.wait_ge(logit_steps[l], q4 + 4)
                                nc.vector.tensor_tensor(tile3(shifted[k]), tile3(logits[k]),
                                                        top.unsqueeze(1).to_broadcast([P, R + 1, H]), ALU.subtract)\
                                    .then_inc(shifted_ready[l], 1)
                                dve.wait_ge(probs_ready[l], q)
                                dve.wait_ge(acc_moved[l], q)
                                nc.vector.tensor_tensor(
                                    weighted[k][:, :, 0:w].rearrange("p s (h d) -> p s h d", h=H),
                                    slots(l, k)[:, :, c["vc"]:c["vc"] + w].rearrange("p s (h d) -> p s h d", h=H),
                                    tile3(probs[k]).unsqueeze(3).to_broadcast([P, R + 1, H, c["dv"]]), ALU.mult)\
                                    .then_inc(weighted_ready[l][k], 1)
                            with dve.If(((i & 3) + 1) >> 2):
                                n = runs_done + (i >> 2)
                                nc.vector.tensor_scalar(degnow[:, :], degnow[:, :], float(-SLOTS), None, ALU.add)\
                                    .then_inc(degree_now[l], 1)
                                dve.wait_ge(degree_now[l], b + n + 2)
                                dve.wait_ge(more_arrived[l], n * 16 + 16)
                                mask_run(more, b + n + 2)
                                dve.wait_ge(runs_taken[l], b + n + 3)
                                dve.sem_inc(waits_done_dve, 1)

            def layer_norm(out_ap, in_ap, n, link, done, var_sem, std_sem, out_sem=None):
                link(nc.vector.bn_stats(st[:, n, :], in_ap))
                dve.sem_inc(waits_done_dve, 1)
                nc.vector.bn_aggr(mv[:, n, :], st[:, n, :]).then_inc(var_sem, 1)
                dve.wait_ge(std_sem, done + 1)
                link(nc.vector.reciprocal(std[:, n, 1:2], std[:, n, 0:1]))
                last = nc.vector.tensor_scalar(out_ap, in_ap, mv[:, n, 0:1], std[:, n, 1:2], ALU.subtract, ALU.mult)
                if out_sem is None:
                    link(last)
                else:
                    last.then_inc(out_sem, 1)

            class Steps:
                def __init__(self, s, it, each, base=0):
                    self.s, self.start, self.each, self.n = s, it * each + base, each, 0

                def __call__(self, ins):
                    self.n += 1
                    ins.then_inc(self.s, 1)
                    dve.wait_ge(self.s, self.start + self.n)

            def normalise(l, b, link):
                H, dv = LAYERS[l]["H"], LAYERS[l]["dv"]
                rows = sums[:, bass.ds(b, 1), 0:H * dv].rearrange("p b (h d) -> p (b h) d", h=H)
                nc.vector.tensor_scalar(norm[:, 2, 0:1], bt[l][:, bass.ds(b, 1), 2], 1.0, None, ALU.min)
                link(nc.vector.tensor_scalar(norm[:, 0, 0:H], rows[:, :, dv - 1], 1e-30, None, ALU.max))
                link(nc.vector.reciprocal(norm[:, 1, 0:H], norm[:, 0, 0:H]))
                link(nc.vector.tensor_scalar(norm[:, 3, 0:H], norm[:, 1, 0:H], norm[:, 2, 0:1], None, ALU.mult))
                return nc.vector.tensor_tensor(aggn[:, :].rearrange("p (h d) -> p h d", h=H), rows[:, :, 0:dv - 1],
                                               norm[:, 3, 0:H].unsqueeze(2).to_broadcast([P, H, dv - 1]), ALU.mult)

            def dense_b():
                dve.wait_ge(block_kept[0], BLOCKS)
                with dve.Fori(0, BLOCKS // 2) as b2:
                    for h in range(2):
                        b = b2 * 2 + h
                        with dve.If(b2):
                            dve.wait_ge(b_stored[h], b2 * 32)
                            dve.sem_inc(waits_done_dve, 1)
                        link = Steps(dense_chain, b, 10)
                        link(normalise(0, b, link))
                        dve.wait_ge(b_x[h], b2 * 16 + 16)
                        link(nc.vector.scalar_tensor_tensor(pre[:, :], aggn[:, :], 0.0, xg[h][:, 0:D], ALU.max, ALU.add))
                        layer_norm(kx[h][:, D:2 * D], pre[:, :], 0, link, b * 2, variance_ready, root_ready)
                        layer_norm(zn[:, :], kx[h][:, D:2 * D], 1, link, b * 2 + 1, variance_ready, root_ready, normed)
                        dve.wait_ge(b_qkv, b + 1)
                        nc.vector.tensor_tensor(qv[h][:, 0:D], bank[5][:, 0:D], qkv_bias[:, 0:D], ALU.add)
                        nc.vector.scalar_tensor_tensor(kx[h][:, 0:D], bank[5][:, D:2 * D], 1.0 / 16, qkv_bias[:, D:2 * D],
                                                       ALU.mult, ALU.add)
                        nc.vector.tensor_tensor(qv[h][:, D:W1].rearrange("p (h d) -> p h d", h=8)[:, :, 0:32],
                                                bank[6][:, 0:D].rearrange("p (h d) -> p h d", h=8),
                                                qkv_bias[:, 2 * D:3 * D].rearrange("p (h d) -> p h d", h=8), ALU.add)\
                            .then_inc(b_rows, 1)
                        dve.wait_ge(b_rows, b + 1)
                        dve.sem_inc(waits_done_dve, 1)
                        assert link.n == link.each, link.n

            def dense_c():
                dve.wait_ge(block_kept[1], BLOCKS)
                with dve.Fori(0, BLOCKS // 2) as b2:
                    for h in range(2):
                        b = b2 * 2 + h
                        with dve.If(b2):
                            dve.wait_ge(c_stored[h], b2 * 16)
                            dve.sem_inc(waits_done_dve, 1)
                        link = Steps(dense_chain, b, 11, 10 * BLOCKS)
                        normalise(1, b, link).then_inc(normed, 1)
                        dve.wait_ge(c_x[h], b2 * 16 + 16)
                        link(nc.vector.tensor_tensor(pre[:, :], xg[h][:, D:2 * D], in_bias[:, :], ALU.add))
                        dve.wait_ge(c_proj, b + 1)
                        link(nc.vector.tensor_tensor(mid[:, :], bank[4][:, 0:D], pre[:, :], ALU.add))
                        layer_norm(zn[:, :], mid[:, :], 0, link, b * 2 + 2 * BLOCKS, variance_ready, root_ready, normed)
                        link(nc.vector.tensor_tensor(pre[:, :], mid[:, :], f2_bias[:, :], ALU.add))
                        link(nc.vector.tensor_tensor(mid[:, :], pre[:, :], xg[h][:, D:2 * D], ALU.add))
                        dve.wait_ge(c_down, b + 1)
                        nc.vector.tensor_tensor(pre[:, :], bank[7][:, 0:D], mid[:, :], ALU.add).then_inc(c_res, 1)
                        dve.wait_ge(c_res, b + 1)
                        layer_norm(outrow[h][:, :], pre[:, :], 1, link, b * 2 + (2 * BLOCKS + 1), variance_ready, root_ready, c_out)
                        dve.wait_ge(c_out, b + 1)
                        dve.sem_inc(waits_done_dve, 1)
                        assert link.n == link.each, link.n

            for l in (0, 1):
                dve.sem_inc(acc_moved[l], 1)
            rows_before()
            histogram(0)
            offsets(0)
            sort_by_degree(0)
            rank_edges(0)
            edge_records()
            histogram(1)
            offsets(1)
            sort_by_degree(1)
            with dve.If(dve.value_load(unsorted[0:1, 0:1], min_val=0, max_val=1)):
                rank_edges(1)
            aggregate(0)
            dense_b()
            aggregate(1)
            dense_c()


_INS = ["x", "src", "dst", "edge_attr_8", "edge_attr_8_n2", "L0_gnn_W", "L0_gnn_a", "L1_gnn_ln1_g", "L1_gnn_ln1_b",
        "L1_gnn_qkv_w", "L1_gnn_qkv_b", "L1_gnn_res_ln_g", "L1_gnn_res_ln_b", "L1_gnn_inproj_w", "L1_gnn_inproj_b",
        "L1_gnn_ffn1_w", "L1_gnn_ffn1_b", "L1_gnn_ffn2_w", "L1_gnn_ffn2_b"]


def kernel(**inputs):
    import numpy as _np
    import concourse.bacc as _bacc
    from concourse import mybir as _mybir
    from concourse.bass_utils import run_bass_kernel_spmd as _run

    nc = _bacc.Bacc("TRN2", target_bir_lowering=False, num_devices=1)
    arrays, args = {}, []
    for name in _INS:
        arr = _np.ascontiguousarray(inputs[name])
        arrays[f"in_{name}"] = arr
        args.append(nc.dram_tensor(f"in_{name}", arr.shape, _mybir.dt.from_np(arr.dtype), kind="ExternalInput").ap())
    args.append(nc.dram_tensor("out_0", (N, D), _mybir.dt.float32, kind="ExternalOutput").ap())
    build(nc, *args)
    r = _run(nc, [arrays], core_ids=[0])
    return r.results[0]["out_0"]
```
